# Optimizing a Trainium2 kernel written in Bass

```python
import numpy as np
import jax
import jax.numpy as jnp

def _softmax(x, axis=-1):
    return jax.nn.softmax(x, axis=axis)
def _gelu(x):
    return jax.nn.gelu(x, approximate=True)
def _silu(x):
    return jax.nn.silu(x)
def _sigmoid(x):
    return jax.nn.sigmoid(x)
def _layernorm(x, axis=-1, eps=1e-5):
    m = jnp.mean(x, axis=axis, keepdims=True)
    v = jnp.var(x, axis=axis, keepdims=True)
    return (x - m) / jnp.sqrt(v + eps)
def _scatter_add(tgt, idx, src, axis=0):
    return tgt.at[idx].add(src)
def _segment_sum(src, seg, n):
    return jax.ops.segment_sum(src, seg, n)

kernel_name = 'mk_conv_preact_d4_conv_nchw64_45350d'

def setup_inputs(seed: int = 0):
    np.random.seed(seed)
    _w = jnp.asarray
    def _rec_inputs():
        import jax
        import jax.numpy as jnp
        _gk = jax.random.key(seed)
        x = -8.268e-05 + 0.9999 * jax.random.normal(jax.random.fold_in(_gk, 1), (32, 64, 112, 112), jnp.float32)
        return x
    x = _rec_inputs()
    def _L0_conv_setup():
        import jax, jax.numpy as jnp
        import numpy as np
        import math
        B, C_IN, C_OUT, H, W = (64, 64, 64, 112, 112)
        A_MAX, T = (3, 8)

        def _spiral_offsets(c_in, a_max, t):
            offs = []
            for c in range(c_in):
                if a_max == 0:
                    dh, dw = (0, 0)
                else:
                    if 0 <= c < c_in / 2:
                        ac = math.floor(2 * a_max / c_in * c)
                    else:
                        ac = math.floor(2 * a_max - 2 * a_max / c_in * c)
                    angle = c * 2 * math.pi / t
                    dh = round(ac * math.cos(angle))
                    dw = round(ac * math.sin(angle))
                offs.append((dh, dw))
            return np.asarray(offs, dtype=np.int32)
        key = jax.random.key(seed)
        kx, kw = jax.random.split(key)
        x = jax.random.normal(kx, (B, C_IN, H, W), dtype=jnp.float32)
        weight = jax.random.normal(kw, (C_IN, C_OUT), dtype=jnp.float32)
        bias = jnp.zeros((C_OUT,), dtype=jnp.float32)
        offsets = jnp.asarray(_spiral_offsets(C_IN, A_MAX, T))
        return {'x': x, 'weight': weight, 'bias': bias, 'offsets': offsets}
    _L0_conv_all = _L0_conv_setup()
    _L0_conv_in = {k: v for k, v in _L0_conv_all.items() if k in ('weight', 'bias', 'offsets', )}
    del _L0_conv_all

    def _L1_conv_setup():
        import jax, jax.numpy as jnp
        import numpy as np
        from jax import lax
        STRIDE = 1
        PAD = 1
        key = jax.random.key(seed)
        k1, k2 = jax.random.split(key)
        X = jax.random.normal(k1, (16, 64, 256, 256), dtype=jnp.float32)
        K = jax.random.normal(k2, (3, 3), dtype=jnp.float32)
        return {'X': X, 'K': K}
    _L1_conv_all = _L1_conv_setup()
    _L1_conv_in = {k: v for k, v in _L1_conv_all.items() if k in ('K', )}
    del _L1_conv_all

    def _L2_conv_setup():
        import jax, jax.numpy as jnp
        import numpy as np
        from jax import lax
        EPS = 1e-05

        def _conv3x3(x, w, b):
            y = lax.conv_general_dilated(x, w, window_strides=(1, 1), padding='SAME', dimension_numbers=('NCHW', 'OIHW', 'NCHW'))
            return y + b[None, :, None, None]

        def _bn(x, g, be, m, v):
            inv = g / jnp.sqrt(v + EPS)
            return x * inv[None, :, None, None] + (be - m * inv)[None, :, None, None]

        def _haar_edge(x):
            B, C, H, W = x.shape
            xr = x.reshape(B, C, H // 2, 2, W // 2, 2)
            a = xr[:, :, :, 0, :, 0]
            b = xr[:, :, :, 0, :, 1]
            c = xr[:, :, :, 1, :, 0]
            d = xr[:, :, :, 1, :, 1]
            return (3.0 * a - b - c - d) * 0.5
        key = jax.random.key(seed)
        ks = jax.random.split(key, 4)
        B, C, H, W = (8, 64, 256, 256)
        x = jax.random.normal(ks[0], (B, C, H, W), dtype=jnp.float32)
        w1 = jax.random.normal(ks[1], (C, C, 3, 3), dtype=jnp.float32) * 0.05
        w2 = jax.random.normal(ks[2], (C, C, 3, 3), dtype=jnp.float32) * 0.05
        a_prelu = jnp.full((1,), 0.25, dtype=jnp.float32)
        zeros = jnp.zeros((C,), dtype=jnp.float32)
        ones = jnp.ones((C,), dtype=jnp.float32)
        return {'x': x, 'w1': w1, 'b1': zeros, 'g1': ones, 'be1': zeros, 'm1': zeros, 'v1': ones, 'a_prelu': a_prelu, 'w2': w2, 'b2': zeros, 'g2': ones, 'be2': zeros, 'm2': zeros, 'v2': ones}
    _L2_conv_all = _L2_conv_setup()
    _L2_conv_in = {k: v for k, v in _L2_conv_all.items() if k in ('w1', 'b1', 'g1', 'be1', 'm1', 'v1', 'a_prelu', 'w2', 'b2', 'g2', 'be2', 'm2', 'v2', )}
    del _L2_conv_all

    def _L3_conv_setup():
        import jax, jax.numpy as jnp
        import numpy as np
        MASK_RADIUS = 30.0

        def _fft_mask(height, width, mode):
            cht, cwt = (height // 2, width // 2)
            fy, fx = jnp.meshgrid(jnp.arange(height), jnp.arange(width // 2 + 1), indexing='ij')
            dist = jnp.sqrt((fx - cwt).astype(jnp.float32) ** 2 + (fy - cht).astype(jnp.float32) ** 2)
            if mode == 'high':
                return (dist > MASK_RADIUS).astype(jnp.float32)
            return (dist <= MASK_RADIUS).astype(jnp.float32)
        key = jax.random.key(seed)
        k1, k2, k3 = jax.random.split(key, 3)
        B, Cin, Cout, H, W, K = (4, 64, 64, 128, 128, 3)
        x = jax.random.normal(k1, (B, Cin, H, W), dtype=jnp.float32)
        weight = jax.random.normal(k2, (Cout, Cin, K, K), dtype=jnp.float32) * 0.1
        bias = jax.random.normal(k3, (Cout,), dtype=jnp.float32) * 0.1
        return {'x': x, 'weight': weight, 'bias': bias}
    _L3_conv_all = _L3_conv_setup()
    _L3_conv_in = {k: v for k, v in _L3_conv_all.items() if k in ('weight', 'bias', )}
    del _L3_conv_all

    return {
        "x": x,
        "L0_conv_weight": _L0_conv_in["weight"],
        "L0_conv_bias": _L0_conv_in["bias"],
        "L0_conv_offsets": _L0_conv_in["offsets"],
        "L1_conv_K": _L1_conv_in["K"],
        "L2_conv_w1": _L2_conv_in["w1"],
        "L2_conv_b1": _L2_conv_in["b1"],
        "L2_conv_g1": _L2_conv_in["g1"],
        "L2_conv_be1": _L2_conv_in["be1"],
        "L2_conv_m1": _L2_conv_in["m1"],
        "L2_conv_v1": _L2_conv_in["v1"],
        "L2_conv_a_prelu": _L2_conv_in["a_prelu"],
        "L2_conv_w2": _L2_conv_in["w2"],
        "L2_conv_b2": _L2_conv_in["b2"],
        "L2_conv_g2": _L2_conv_in["g2"],
        "L2_conv_be2": _L2_conv_in["be2"],
        "L2_conv_m2": _L2_conv_in["m2"],
        "L2_conv_v2": _L2_conv_in["v2"],
        "L3_conv_weight": _L3_conv_in["weight"],
        "L3_conv_bias": _L3_conv_in["bias"],
    }

def reference(x, L0_conv_weight, L0_conv_bias, L0_conv_offsets, L1_conv_K, L2_conv_w1, L2_conv_b1, L2_conv_g1, L2_conv_be1, L2_conv_m1, L2_conv_v1, L2_conv_a_prelu, L2_conv_w2, L2_conv_b2, L2_conv_g2, L2_conv_be2, L2_conv_m2, L2_conv_v2, L3_conv_weight, L3_conv_bias):
    import jax
    import jax.numpy as jnp
    def _L0_conv_ref(x, weight, bias, offsets):
        import jax, jax.numpy as jnp
        import numpy as np
        import math
        B, C_IN, C_OUT, H, W = (64, 64, 64, 112, 112)
        A_MAX, T = (3, 8)

        def _spiral_offsets(c_in, a_max, t):
            offs = []
            for c in range(c_in):
                if a_max == 0:
                    dh, dw = (0, 0)
                else:
                    if 0 <= c < c_in / 2:
                        ac = math.floor(2 * a_max / c_in * c)
                    else:
                        ac = math.floor(2 * a_max - 2 * a_max / c_in * c)
                    angle = c * 2 * math.pi / t
                    dh = round(ac * math.cos(angle))
                    dw = round(ac * math.sin(angle))
                offs.append((dh, dw))
            return np.asarray(offs, dtype=np.int32)
        P = A_MAX
        b, c, h, w = x.shape
        x_padded = jnp.pad(x, ((0, 0), (0, 0), (P, P), (P, P)))
        h_idx = (P + offsets[:, 0])[:, None] + jnp.arange(h)[None, :]
        w_idx = (P + offsets[:, 1])[:, None] + jnp.arange(w)[None, :]
        c_idx = jnp.arange(c)
        sampled = x_padded[:, c_idx[:, None, None], h_idx[:, :, None], w_idx[:, None, :]]
        out = jnp.einsum('bchw,co->bohw', sampled, weight) + bias[None, :, None, None]
        return out

    def _L1_conv_ref(X, K):
        import jax, jax.numpy as jnp
        import numpy as np
        from jax import lax
        STRIDE = 1
        PAD = 1
        B, C, H, W = X.shape
        x = X.reshape(B * C, 1, H, W)
        k = K[None, None, :, :]
        out = lax.conv_general_dilated(x, k, window_strides=(STRIDE, STRIDE), padding=[(PAD, PAD), (PAD, PAD)], dimension_numbers=('NCHW', 'OIHW', 'NCHW'))
        Ho, Wo = (out.shape[2], out.shape[3])
        return out.reshape(B, C, Ho, Wo)

    def _L2_conv_ref(x, w1, b1, g1, be1, m1, v1, a_prelu, w2, b2, g2, be2, m2, v2):
        import jax, jax.numpy as jnp
        import numpy as np
        from jax import lax
        EPS = 1e-05

        def _conv3x3(x, w, b):
            y = lax.conv_general_dilated(x, w, window_strides=(1, 1), padding='SAME', dimension_numbers=('NCHW', 'OIHW', 'NCHW'))
            return y + b[None, :, None, None]

        def _bn(x, g, be, m, v):
            inv = g / jnp.sqrt(v + EPS)
            return x * inv[None, :, None, None] + (be - m * inv)[None, :, None, None]

        def _haar_edge(x):
            B, C, H, W = x.shape
            xr = x.reshape(B, C, H // 2, 2, W // 2, 2)
            a = xr[:, :, :, 0, :, 0]
            b = xr[:, :, :, 0, :, 1]
            c = xr[:, :, :, 1, :, 0]
            d = xr[:, :, :, 1, :, 1]
            return (3.0 * a - b - c - d) * 0.5
        edge = _haar_edge(x)
        edge = jax.image.resize(edge, x.shape, method='bilinear')
        h = _bn(_conv3x3(x, w1, b1), g1, be1, m1, v1)
        h = jnp.where(h > 0, h, a_prelu[0] * h)
        h = _bn(_conv3x3(h, w2, b2), g2, be2, m2, v2)
        return x + h + edge

    def _L3_conv_ref(x, weight, bias):
        import jax, jax.numpy as jnp
        import numpy as np
        MASK_RADIUS = 30.0

        def _fft_mask(height, width, mode):
            cht, cwt = (height // 2, width // 2)
            fy, fx = jnp.meshgrid(jnp.arange(height), jnp.arange(width // 2 + 1), indexing='ij')
            dist = jnp.sqrt((fx - cwt).astype(jnp.float32) ** 2 + (fy - cht).astype(jnp.float32) ** 2)
            if mode == 'high':
                return (dist > MASK_RADIUS).astype(jnp.float32)
            return (dist <= MASK_RADIUS).astype(jnp.float32)
        B, Cin, H, W = x.shape
        x = x.astype(jnp.float32)
        fft_x = jnp.fft.rfft2(x)
        fft_x = jnp.fft.fftshift(fft_x, axes=(-2, -1))
        kernel_fft = jnp.fft.rfft2(weight, s=(H, W))
        mask = _fft_mask(H, W, 'high')
        fft_x = fft_x * mask
        fft_out = jnp.einsum('bihw,oihw->bohw', fft_x, kernel_fft)
        out = jnp.fft.irfft2(fft_out, s=(H, W))
        return out + bias[None, :, None, None]

    def _gn(v, G=32, eps=1e-5):
        B_, C_, H_, W_ = v.shape
        g = v.reshape(B_, G, C_ // G, H_, W_)
        m = jnp.mean(g, axis=(2, 3, 4), keepdims=True)
        s = jnp.var(g, axis=(2, 3, 4), keepdims=True)
        return ((g - m) / jnp.sqrt(s + eps)).reshape(v.shape)

    def _ln_c(v, eps=1e-6):
        m = jnp.mean(v, axis=1, keepdims=True)
        s = jnp.var(v, axis=1, keepdims=True)
        return (v - m) / jnp.sqrt(s + eps)

    def _ln_t(v, eps=1e-5):
        m = jnp.mean(v, axis=-1, keepdims=True)
        s = jnp.var(v, axis=-1, keepdims=True)
        return (v - m) / jnp.sqrt(s + eps)

    def _to_tokens(v):
        B_, C_, H_, W_ = v.shape
        return v.reshape(B_, C_, H_ * W_).transpose(0, 2, 1)
    def _from_tokens(t, like):
        B_, C_, H_, W_ = like.shape
        return t.transpose(0, 2, 1).reshape(B_, C_, H_, W_)

    x = x + _L0_conv_ref(_gn(x), L0_conv_weight, L0_conv_bias, L0_conv_offsets)
    x = x + _L1_conv_ref(_gn(x), L1_conv_K)
    x = x + _L2_conv_ref(_gn(x), L2_conv_w1, L2_conv_b1, L2_conv_g1, L2_conv_be1, L2_conv_m1, L2_conv_v1, L2_conv_a_prelu, L2_conv_w2, L2_conv_b2, L2_conv_g2, L2_conv_be2, L2_conv_m2, L2_conv_v2)
    x = x + _L3_conv_ref(_gn(x), L3_conv_weight, L3_conv_bias)
    return x


_drawn_inputs = setup_inputs


def setup_inputs(seed=0):
    import zlib

    import numpy as np

    out = dict(_drawn_inputs(seed))
    spreads = {'L0_conv_bias': (0.0, 0.8),
     'L2_conv_b1': (0.0, 0.8),
     'L2_conv_g1': (1.0, 0.6),
     'L2_conv_be1': (0.0, 0.8),
     'L2_conv_m1': (0.0, 0.692),
     'L2_conv_v1': (1.0, 0.6),
     'L2_conv_b2': (0.0, 0.8),
     'L2_conv_g2': (1.0, 0.6),
     'L2_conv_be2': (0.0, 0.8),
     'L2_conv_m2': (0.0, 0.683),
     'L2_conv_v2': (1.0, 0.6)}
    factors = {'L3_conv_bias': 5.824}
    for name, (base, spread) in spreads.items():
        noise = np.random.default_rng([zlib.crc32(name.encode()), seed]).standard_normal(out[name].shape)
        drawn = base * np.exp(spread * noise) if base else spread * noise
        out[name] = jnp.asarray(drawn.astype(out[name].dtype))
    for name, factor in factors.items():
        out[name] = (out[name] * factor).astype(out[name].dtype)
    return out
```

```python
from contextlib import ExitStack

import numpy as np
import concourse.bass as bass
from concourse import mybir
from concourse.alu_op_type import AluOpType as ALU

F32, F16, I32 = mybir.dt.float32, mybir.dt.float16, mybir.dt.int32
ACT = mybir.ActivationFunctionType

N, C, H, W = 32, 64, 112, 112
HALF = H // 2
HALF1 = HALF + 1
R = 4
NB = R * W
K0 = HALF // R
K1 = K0 + 1
PADS = 4
PITCH = W + PADS
ROW = 2 * PITCH
REACH = 3
SHIFTED = H + 2 * REACH
GUARD = 8
YROW = 2 * (W + 2)
YROWS = H + 4
UNITS = 7
U = 2 * R
EARLY = 4
PLANES = 4
RING = 4
STEPS = C // PLANES + 3
FFTS = C // PLANES
MASKED = 61
EPS = 1e-5
WSCALE = 256.0
KSCALE = 16.0
W2SCALE = 64.0
FFT_AT = 3
L0_AT = 4
X_AT = 2
GN1_AT = 8
L0_WITH = 4
SETUP_V = 21
MSCALE = 8.0


def chunk(k, last=K1 - 1):
    return R * k, (1 if k == last else R)


def unit(u):
    return U * u, (U + 1 if u == UNITS - 1 else U)


def split3_with(k):
    return {12: (10, 11), 13: (12, 13), 14: (14,)}.get(k, (k - 2,) if k >= 2 else ())


def layer0_with(k):
    first = L0_WITH * (k - L0_AT)
    return range(first, min(first + L0_WITH, K0)) if k >= L0_AT else ()


def build(nc, x, offsets, w0, k1, delta, w1, w2, w3, params, average, edge, edge_ends, spectrum,
          mask, out):
    ctx = ExitStack()
    with ctx:
        def sb(name, shape, dt):
            return ctx.enter_context(nc.sbuf_tensor(name, shape, dt))

        def sem(name):
            return ctx.enter_context(nc.semaphore(name))

        shifted = nc.dram_tensor("shifted", (GUARD + C * SHIFTED * ROW + GUARD,), F16, kind="Internal").ap()
        rows3 = nc.dram_tensor("rows3", (C, H + 2, ROW), F16, kind="Internal").ap()
        rowsy = nc.dram_tensor("rowsy", (C, YROWS, YROW), F16, kind="Internal").ap()

        X = sb("X", [128, HALF, W], F32)
        FRONT = PADS
        A = sb("A", [128, FRONT + (HALF + 2) * ROW], F16)
        Hb = sb("Hb", [128, FRONT + (HALF + 2) * ROW], F16)
        X2 = [sb(f"X2_{p}", [128, HALF1, W], F32) for p in range(2)]
        stage = sb("stage", [128, 2, U + 1, ROW], F16)
        planes = sb("planes", [H, RING, PLANES, ROW], F16)
        z1 = sb("z1", [W, 2, 2, NB], F16)
        z2 = sb("z2", [H, 2, 2, PLANES, W], F16)
        zm = sb("zm", [H, 2, PLANES, MASKED], F32)
        z3 = sb("z3", [H, 2, 2, NB], F16)
        ystage = sb("ystage", [H, 2, PLANES, 2, W + 2], F16)
        Y = sb("Y", [128, 2, U + 2, YROW], F16)
        relu = sb("relu", [128, 2, NB], F32)
        leak = sb("leak", [128, 2, NB], F32)
        last_tmp = sb("last_tmp", [128, 2, NB], F32)
        g3 = sb("g3", [128, U, HALF], F32)
        g1 = sb("g1", [128, U, HALF + 2], F32)
        ebuf = sb("ebuf", [128, U, HALF, 2], F32)

        M0 = sb("M0", [128, 128], F32)
        MK = sb("MK", [128, 6 * 128], F32)
        M1 = sb("M1", [128, 6 * 128], F32)
        M3 = sb("M3", [128, 6 * 128], F32)
        FK = sb("FK", [128, 6 * 128], F32)
        D1 = sb("D1", [128, 2 * 128], F32)
        P0w = sb("P0w", [128, 2, 128], F16)
        PKw = sb("PKw", [128, 2, 6 * 128], F16)
        P1w = sb("P1w", [128, 2, 6 * 128], F16)
        P2w = sb("P2w", [128, 2, 6 * 128], F16)
        P3w = sb("P3w", [128, 2, 6 * 128], F16)
        ED = sb("ED", [128, 6, 128], F16)
        EE = sb("EE", [128, 8, 128], F16)
        SP = sb("SP", [H, 4, 2, W], F16)
        MA = sb("MA", [H, MASKED], F32)
        AV = sb("AV", [128, 128], F32)
        PR = sb("PR", [128, 16], F32)
        GN = sb("GN", [128, 4, 16], F32)
        ST = [sb(f"ST{q}", [128, K1 + 1, 6], F32) for q in range(4)]
        OFFI = sb("OFFI", [1, 2 * C], I32)
        OFF = sb("OFF", [1, C], I32)
        OFFB = sb("OFFB", [1, 2 * C], I32)

        PS = [ctx.enter_context(nc.psum_tensor(f"PS{k}", [128, 512], F32)) for k in range(8)]
        CB = 3
        PSS, PF = PS[3], PS[4:8]

        BIAS0, G1, BE1, MM1, V1, B1, G2, BE2, MM2, V2, B2, BIAS3, ALPHA = range(13)
        PC = sb("PC", [128, 16], F32)
        HALFM, S1, BB1, AS1, AB1, S2, BB2, OMA, VE1, VE2, RT1, RT2, ONE, KS, WS = range(15)

        def at(t, size, dims, off=0, p0=0, pn=128):
            return bass.AP(t, p0 * size + off, [[size, pn], *dims])

        ASIZE = FRONT + (HALF + 2) * ROW

        def win(t, s0, n, part, col=0, step=1, w=W, stride=1):
            return at(t, ASIZE, [[ROW * stride, n], [step, w]], FRONT + (s0 + 1) * ROW + part * PITCH + col)

        def slots(t, s0, n, stride=1):
            size = (HALF if t is X else HALF1) * W
            return at(t, size, [[W * stride, n], [1, W]], s0 * W)

        def bank(p, n=NB, w=W, parts=128):
            return bass.AP(p, 0, [[512, parts], [w, n // w], [1, w]])

        const_in = sem("const_in")
        offs_in = sem("offs_in")
        zeroed = sem("zeroed")
        guards_out = sem("guards_out")
        setup_v, setup_p, setup_a = sem("setup_v"), sem("setup_p"), sem("setup_a")
        x_in = [sem(f"x_in{u}") for u in range(UNITS)]
        st0_out = [sem(f"st0_out{p}") for p in range(2)]
        st3_out = [sem(f"st3_out{p}") for p in range(2)]
        gathered = [sem(f"gathered{p}") for p in range(4)]
        planes_in = [sem(f"planes_in{p}") for p in range(RING)]
        y_out = [sem(f"y_out{p}") for p in range(2)]
        y_in = [sem(f"y_in{p}") for p in range(2)]
        out_early = sem("out_early")
        out_late = sem("out_late")
        BN = [14, 14, 16, 16]
        bn = [sem(f"bn{q}") for q in range(4)]
        gv = [sem(f"gv{q}") for q in range(4)]
        gp = [sem(f"gp{q}") for q in range(4)]
        gr = [sem(f"gr{q}") for q in range(4)]
        RS = [2, 2, 7, 2]
        hi = [sem(f"hi{q}") for q in range(4)]
        lo = [sem(f"lo{q}") for q in range(4)]
        TC = [K0, K0, K1, K1]
        fk = sem("fk")
        fh = [sem(f"fh{q}") for q in range(4)]
        fl = [sem(f"fl{q}") for q in range(4)]
        l0_mm, l0_ev = sem("l0_mm"), sem("l0_ev")
        a_free = sem("a_free")
        pads = sem("pads")
        l1_mm, l1_ev = sem("l1_mm"), sem("l1_ev")
        t2_zero = sem("t2_zero")
        c1_mm = sem("c1_mm")
        c1_act = sem("c1_act")
        c1_h, c1_hi, c1_lo = sem("c1_h"), sem("c1_hi"), sem("c1_lo")
        ed_mm = sem("ed_mm")
        ed_act = sem("ed_act")
        ed_add = sem("ed_add")
        c2_mm, c2_ev = sem("c2_mm"), sem("c2_ev")
        c3_mm, c3_ev, c3_add = sem("c3_mm"), sem("c3_ev"), sem("c3_add")
        f_mm = [sem(f"f_mm{s}") for s in range(4)]
        f_hi = [sem(f"f_hi{s}") for s in range(4)]
        f_lo = [sem(f"f_lo{s}") for s in range(4)]
        f_mask = sem("f_mask")
        y_wrap = sem("y_wrap")
        SLOT_UNITS = [4, 3]
        EDGES = 8

        def edges_with(k):
            return {K0 - 2: (UNITS - 2,), K0 - 1: (UNITS - 1, UNITS)}.get(k, (k // 2 - 1,) if k % 2 == 1 and k >= 3 else ())

        def due(i, per, n):
            return i * per + n

        def gather(eng, offset_reg, channels):
            for c in channels:
                eng.reg_load(offset_reg, OFF[0:1, c:c + 1])
                first = eng.snap(offset_reg, min_val=GUARD - REACH, max_val=GUARD + 2 * REACH * ROW + REACH)
                plane = shifted[bass.ds(first + c * SHIFTED * ROW, H * ROW)].rearrange("(j q e) -> q j e", q=2, e=ROW)
                eng.dma_start(bass.AP(A, c * ASIZE + FRONT + ROW, [[C * ASIZE, 2], [ROW, HALF], [1, ROW]]), plane)\
                   .then_inc(gathered[c // 16], 16)

        def program(iteration, tail):
            def run(eng):
                iteration(eng, 0, 0, back=False, front=True)
                with eng.Fori(1, N - 2, 2) as i:
                    iteration(eng, i, 1, back=True, front=True)
                    iteration(eng, i + 1, 0, back=True, front=True)
                iteration(eng, N - 1, 1, back=True, front=False)
                tail(eng, N - 1, 1)
            return run

        zero_planes = at(Hb, ASIZE, [[1, REACH * ROW]], 0, pn=C)
        block = ctx.enter_context(nc.Block())

        @block.sync
        def _(eng):
            def load_x(n, u):
                j0 = U * u
                for par in range(2):
                    src = x[n, :, :, :] if isinstance(n, int) else x[bass.ds(n, 1), :, :, :].rearrange("o c h w -> (o c) h w")
                    src = src.rearrange("c (j q) w -> q c j w", q=2)[par][:, j0:j0 + U, :]
                    eng.dma_start(X[par * C:(par + 1) * C, j0:j0 + U, :], src).then_inc(x_in[u], 16)

            consts = [(M0[:, :], w0), (MK[:, :], k1), (M1[:, :], w1), (M3[:, :], w3), (FK[:, :], w2),
                      (D1[:, :], delta), (PR[:, 0:13], params), (AV[:, :], average), (ED[:, :, :], edge),
                      (EE[:, :, :], edge_ends), (SP[:, :, :, :], spectrum), (MA[:, :], mask)]
            for u in range(UNITS):
                load_x(0, u)
            eng.dma_start(OFFI[:, :], offsets).then_inc(offs_in, 16)
            for dst, src in consts:
                eng.dma_start(dst, src).then_inc(const_in, 16)
            eng.wait_ge(zeroed, 4)
            for r0 in (0, REACH + H):
                eng.dma_start(bass.AP(shifted.tensor, GUARD + r0 * ROW, [[SHIFTED * ROW, C], [1, REACH * ROW]]),
                              zero_planes).then_inc(guards_out, 16)
            for off in (0, GUARD + C * SHIFTED * ROW):
                eng.dma_start(bass.AP(shifted.tensor, off, [[GUARD, 1], [1, GUARD]]),
                              at(Hb, ASIZE, [[1, GUARD]], 0, pn=1)).then_inc(guards_out, 16)

            offset_reg = eng.alloc_register("spatial_offset_even")

            def store_t0(n, u):
                eng.wait_ge(lo[0], due(n, TC[0], 2 * u + 2))
                for par in range(2):
                    dst = bass.AP(shifted.tensor, GUARD + (REACH + 2 * U * u + par) * ROW,
                                  [[SHIFTED * ROW, C], [2 * ROW, U], [1, ROW]])
                    eng.dma_start(dst, stage[par * C:(par + 1) * C, u % 2, 0:U, :]).then_inc(st0_out[u % 2], 16)

            def load_planes(b, g):
                if g - RING + 1 > 0:
                    eng.wait_ge(f_mm[0], due(b, FFTS, g - RING + 1))
                eng.dma_start(planes[:, g % RING, :, :],
                              rows3[PLANES * g:PLANES * (g + 1), 1:H + 1, :].rearrange("c h e -> h c e"))\
                   .then_inc(planes_in[g % RING], 16)

            def store_y(b, g):
                eng.wait_ge(y_wrap, due(b, FFTS, g + 1))
                src = ystage[:, g % 2, :, :, :].rearrange("h c p e -> h c (p e)")
                dst = rowsy[PLANES * g:PLANES * (g + 1), :, :].rearrange("c h e -> h c e")
                eng.dma_start(dst[3:H + 3], src).then_inc(y_out[g % 2], 16)
                eng.dma_start(dst[0:3], src[H - 3:H]).then_inc(y_out[g % 2], 16)
                eng.dma_start(dst[H + 3:H + 4], src[0:1]).then_inc(y_out[g % 2], 16)

            def store_t3(i, u):
                eng.wait_ge(lo[3], due(i, TC[3], min(2 * u + 2, K1) if u < UNITS - 1 else K1))
                s0, n = unit(u)
                for par in range(2):
                    dst = bass.AP(rows3.tensor, (2 * s0 + (1 - par)) * ROW, [[(H + 2) * ROW, C], [2 * ROW, n], [1, ROW]])
                    eng.dma_start(dst, stage[par * C:(par + 1) * C, u % 2, 0:n, :]).then_inc(st3_out[u % 2], 16)

            def store_out(b, buf, u):
                eng.wait_ge(c3_add, due(b, K1, 2 * u + 2 if u < UNITS - 1 else K1))
                s0, n = unit(u)
                dst = out[b, :, :, :] if isinstance(b, int) else out[bass.ds(b, 1), :, :, :].rearrange("o c h w -> (o c) h w")
                e1 = min(s0 + n, HALF)
                stored = out_early if u < EARLY else out_late
                eng.dma_start(dst.rearrange("c (j q) w -> q c j w", q=2)[0][:, s0:e1, :],
                              X2[buf][0:C, s0:e1, :]).then_inc(stored, 16)
                o0 = max(s0, 1)
                eng.dma_start(dst.rearrange("c (j q) w -> q c j w", q=2)[1][:, o0 - 1:s0 + n - 1, :],
                              X2[buf][C:2 * C, o0:s0 + n, :]).then_inc(stored, 16)

            def t3_stored(i):
                for p in range(2):
                    eng.wait_ge(st3_out[p], due(i, 32 * SLOT_UNITS[p], 32 * SLOT_UNITS[p]))

            def front_done(n):
                for p in range(2):
                    eng.wait_ge(st0_out[p], due(n, 32 * SLOT_UNITS[p], 32 * SLOT_UNITS[p]))

            def spectrum_step(b, s):
                if s + RING < FFTS:
                    load_planes(b, s + RING)
                if s >= 3:
                    store_y(b, s - 3)

            def iteration(eng, i, buf, back, front):
                n, b = i + 1, i - 1
                for s in range(STEPS):
                    if back:
                        spectrum_step(b, s)
                    if front and X_AT <= s < X_AT + UNITS:
                        if s == X_AT:
                            eng.wait_ge(lo[1], due(i, TC[1], TC[1]))
                        load_x(n, s - X_AT)
                if front:
                    for p in range(4):
                        eng.wait_ge(gathered[p], due(i, 256, 256))
                    for u in range(UNITS):
                        store_t0(n, u)
                    front_done(n)
                    eng.wait_ge(ed_mm, due(i, EDGES, EDGES))
                    eng.wait_ge(c1_mm, due(i, K0, K0))
                    eng.sem_inc(a_free, 1)
                    gather(eng, offset_reg, range(0, C, 2))
                for k in range(K1):
                    if k == 3 and back:
                        eng.wait_ge(f_mm[0], due(b, FFTS, FFTS))
                    for c in split3_with(k):
                        if c == K1 - 1 or c % 2 == 1 and c < K1 - 2:
                            store_t3(i, min(c // 2, UNITS - 1))
                    if back and k % 2 == 1 and k >= 5 and (k - 5) // 2 < EARLY:
                        store_out(b, 1 - buf, (k - 5) // 2)
                t3_stored(i)
                for g in range(RING):
                    load_planes(i, g)
                if back:
                    for u in range(EARLY, UNITS):
                        store_out(b, 1 - buf, u)

            def tail(eng, b, buf):
                for s in range(STEPS):
                    spectrum_step(b, s)
                for u in range(UNITS):
                    store_out(b, buf, u)
                eng.wait_ge(out_early, 32 * EARLY * N)
                eng.wait_ge(out_late, 1 + 32 * (UNITS - EARLY) * N)

            eng.sem_inc(out_late, 1)
            eng.wait_ge(guards_out, 64)
            for u in range(UNITS):
                store_t0(0, u)
            front_done(0)
            eng.wait_ge(setup_v, SETUP_V)
            eng.sem_inc(a_free, 1)
            gather(eng, offset_reg, range(0, C, 2))
            program(iteration, tail)(eng)

        @block.tensor
        def _(eng):
            def products(dst, terms, opens=True):
                for t, (lhs, rhs) in enumerate(terms):
                    mm = nc.tensor.matmul(dst, lhs, rhs, start=opens and t == 0, stop=t == len(terms) - 1)
                return mm

            def three(lhs_hi, lhs_lo, rhs_hi, rhs_lo):
                return [(lhs_hi, rhs_hi), (lhs_hi, rhs_lo), (lhs_lo, rhs_hi)]

            def conv_terms(w, rhs):
                terms = []
                for dx in range(3):
                    for which in range(2):
                        m = (dx * 2 + which) * 128
                        terms += three(w[:, 0, m:m + 128], w[:, 1, m:m + 128], rhs(which, dx, 0), rhs(which, dx, 1))
                return terms

            def layer0(i, k):
                if k == 0:
                    for p in range(4):
                        eng.wait_ge(gathered[p], due(i, 256, 256))
                    eng.wait_ge(fl[0], due(i, 1, 1))
                if k >= 4:
                    eng.wait_ge(l0_ev, due(i, K0, k - 3))
                products(bank(PF[k % 4]), three(P0w[:, 0, :], P0w[:, 1, :], win(A, R * k, R, 0), win(A, R * k, R, 1)))\
                    .then_inc(l0_mm, 1)

            def average(q, i, step):
                eng.wait_ge(gv[q], due(i, 6, 1 if step == 0 else 5))
                col = 2 * q + step
                src = GN[:, q, 0:1] if step == 0 else GN[:, q, 5:6]
                nc.tensor.matmul(PSS[:, col:col + 1], AV[:, :], src, start=True, stop=True).then_inc(gp[q], 1)

            def layer1(i, k):
                s0, n = chunk(k)
                if k == 0:
                    eng.wait_ge(fl[1], due(i, 1, 1))
                    eng.wait_ge(pads, due(i, 3, 3))
                eng.wait_ge(lo[1], due(i, TC[1], min(k + 1, K0)))
                if k >= CB:
                    eng.wait_ge(l1_ev, due(i, K1, k - CB + 1))
                products(bank(PS[k % CB], n * W), conv_terms(PKw, lambda which, dx, part: win(A, s0 - 1 + which, n, part, dx - 1)))\
                    .then_inc(l1_mm, 1)

            def conv1(i, k):
                s0 = R * k
                if k == 0:
                    eng.wait_ge(fl[2], due(i, 1, 1))
                    eng.wait_ge(t2_zero, due(i, 2, 1))
                if k == K0 - 1:
                    eng.wait_ge(t2_zero, due(i, 2, 2))
                eng.wait_ge(lo[2], due(i, TC[2], min(k + 2, K1)))
                if k >= CB:
                    eng.wait_ge(c1_act, due(i, 2 * K0, 2 * (k - CB + 1)))
                products(bank(PS[k % CB]), conv_terms(P1w, lambda which, dx, part: win(A, s0 + which, R, part, dx - 1)))\
                    .then_inc(c1_mm, 1)

            def edges(i, e):
                p = PF[e % 4]
                if e >= 4:
                    eng.wait_ge(ed_act, due(i, 5 * EDGES, 5 * (e - 4) + 5))
                if e < UNITS:
                    s0 = U * e + 1
                    n = min(U, HALF - s0)
                    terms = [(ED[:, 2 * which + col, :], win(A, s0 - 1 + which, n, part, col, 2, HALF))
                             for which in range(3) for col in range(2) for part in range(2)]
                    products(bank(p, n * HALF, HALF), terms).then_inc(ed_mm, 1)
                    return
                for end, (first, second) in enumerate(((0, 1), (HALF - 1, HALF))):
                    terms = [(EE[:, 4 * end + 2 * at_ + col, :], win(A, s, 1, part, col, 2, HALF))
                             for at_, s in enumerate((first, second)) for col in range(2) for part in range(2)]
                    mm = products(bass.AP(p, end * HALF, [[512, 128], [1, HALF]]), terms)
                mm.then_inc(ed_mm, 1)

            def conv2(i, k):
                s0, n = chunk(k)
                eng.wait_ge(c1_lo, due(i, K0, min(k + 1, K0)))
                if k < 2:
                    eng.wait_ge(c1_act, due(i, 2 * K0, 2 * (K0 - 1 + k)))
                if k >= CB:
                    eng.wait_ge(c2_ev, due(i, K1, k - CB + 1))
                products(bank(PS[k % CB], n * W), conv_terms(P2w, lambda which, dx, part: win(Hb, s0 - 1 + which, n, part, dx - 1)))\
                    .then_inc(c2_mm, 1)

            def conv3(b, k):
                s0, n = chunk(k)
                u = min(k // 2, UNITS - 1)
                if k == 0:
                    eng.wait_ge(fl[3], due(b, 1, 1))
                if k % 2 == 0 and k // 2 < UNITS:
                    eng.wait_ge(y_in[u % 2], due(b, 32 * SLOT_UNITS[u % 2], 32 * (u // 2 + 1)))
                if k >= CB:
                    eng.wait_ge(c3_ev, due(b, K1, k - CB + 1))

                def rhs(which, dx, part):
                    off = (u % 2) * (U + 2) * YROW + (s0 - U * u + which) * YROW + part * (W + 2) + 2 - dx
                    return at(Y, 2 * (U + 2) * YROW, [[YROW, n], [1, W]], off)
                products(bank(PS[k % CB], n * W), conv_terms(P3w, rhs)).then_inc(c3_mm, 1)

            def spectrum_step(b, s):
                g = s
                if g < FFTS:
                    eng.wait_ge(planes_in[g % RING], due(b, 64, 16 * (g // RING + 1)))
                    if g > 0:
                        eng.wait_ge(f_lo[0], due(b, FFTS, g))
                    for c in range(PLANES):
                        pl = planes[:, g % RING, c, :]
                        mm = products(PF[0][0:W, c * W:(c + 1) * W],
                                      [(pl[:, 0:W], SP[:, 0, 0, :]), (pl[:, 0:W], SP[:, 0, 1, :]),
                                       (pl[:, PITCH:PITCH + W], SP[:, 0, 0, :])])
                    mm.then_inc(f_mm[0], 1)
                g = s - 1
                if 0 <= g < FFTS:
                    if 2 * g > 0:
                        eng.wait_ge(f_lo[1], due(b, 2 * FFTS, 2 * g))
                    eng.wait_ge(f_lo[0], due(b, FFTS, g + 1))
                    products(PF[1][0:H, 0:NB], three(SP[:, 1, 0, :], SP[:, 1, 1, :], z1[:, g % 2, 0, :], z1[:, g % 2, 1, :]))\
                        .then_inc(f_mm[1], 1)
                g = s - 2
                if 0 <= g < FFTS:
                    if g > 0:
                        eng.wait_ge(f_lo[2], due(b, FFTS, g))
                    eng.wait_ge(f_lo[1], due(b, 2 * FFTS, 2 * g + 2))
                    for c in range(PLANES):
                        mm = products(PF[2][0:H, c * W:(c + 1) * W],
                                      [(z2[:, g % 2, 0, c, :], SP[:, 2, 0, :]), (z2[:, g % 2, 0, c, :], SP[:, 2, 1, :]),
                                       (z2[:, g % 2, 1, c, :], SP[:, 2, 0, :])])
                    mm.then_inc(f_mm[2], 1)
                g = s - 3
                if 0 <= g < FFTS:
                    if g > 0:
                        eng.wait_ge(f_lo[3], due(b, FFTS, g))
                    eng.wait_ge(f_lo[2], due(b, FFTS, g + 1))
                    products(PF[3][0:H, 0:NB], three(SP[:, 3, 0, :], SP[:, 3, 1, :], z3[:, g % 2, 0, :], z3[:, g % 2, 1, :]))\
                        .then_inc(f_mm[3], 1)

            def iteration(eng, i, buf, back, front):
                n, b = i + 1, i - 1
                for k in range(K1):
                    layer1(i, k)
                    if back and k == FFT_AT:
                        eng.wait_ge(l0_ev, due(i, K0, K0))
                    if back and k >= FFT_AT:
                        spectrum_step(b, k - FFT_AT)
                if back:
                    spectrum_step(b, STEPS - 7)
                average(2, i, 0)
                if back:
                    spectrum_step(b, STEPS - 6)
                average(2, i, 1)
                if back:
                    spectrum_step(b, STEPS - 5)
                    spectrum_step(b, STEPS - 4)
                for k in range(K0):
                    conv1(i, k)
                    if back and k < 3:
                        spectrum_step(b, STEPS - 3 + k)
                    if back and k == 3:
                        for s in range(4):
                            eng.wait_ge(f_lo[s], due(b, FFTS * (2 if s == 1 else 1), FFTS * (2 if s == 1 else 1)))
                    for e in edges_with(k):
                        edges(i, e)
                    if front and k == 1:
                        average(0, n, 0)
                    if front and k == 3:
                        average(0, n, 1)
                for k in range(K1):
                    conv2(i, k)
                if front:
                    eng.wait_ge(gv[0], due(n, 6, 6))
                eng.wait_ge(c2_ev, due(i, K1, K1))
                for k in range(K1):
                    if back:
                        conv3(b, k)
                    if k == 1:
                        average(3, i, 0)
                    if k == 2:
                        average(3, i, 1)
                    if front:
                        if k == L0_AT:
                            eng.wait_ge(ed_act, due(i, 5 * EDGES, 5 * EDGES))
                        for c in layer0_with(k):
                            layer0(n, c)
                        if k == GN1_AT:
                            eng.wait_ge(gv[3], due(i, 6, 6))
                            average(1, n, 0)
                        if k == GN1_AT + 1:
                            average(1, n, 1)

            def tail(eng, b, buf):
                eng.wait_ge(ed_act, due(b, 5 * EDGES, 5 * EDGES))
                for s in range(STEPS):
                    spectrum_step(b, s)
                for k in range(K1):
                    conv3(b, k)

            eng.wait_ge(const_in, 16 * 12)
            average(0, 0, 0)
            average(0, 0, 1)
            for k in range(K0):
                layer0(0, k)
            average(1, 0, 0)
            average(1, 0, 1)
            program(iteration, tail)(eng)

        @block.scalar
        def _(eng):
            offset_reg = eng.alloc_register("spatial_offset_odd")

            def act(dst, src, **kw):
                return nc.scalar.activation(dst, src, ACT.Identity, **kw)

            def split_hi(q, i, k, src, dst):
                if k == 0:
                    eng.wait_ge(gv[q], due(i, 6, 2))
                act(dst, src, bias=GN[:, q, 2:3]).then_inc(hi[q], 1)

            def staged(k, n, part):
                u = min(k // 2, UNITS - 1)
                return stage[:, u % 2, R * k - U * u:R * k - U * u + n, part * PITCH:part * PITCH + W]

            def split0(n, k, first=False):
                u = k // 2
                if k % 2 == 0:
                    eng.wait_ge(x_in[u], due(n, 32, 32))
                if k % 2 == 0:
                    if u < 2:
                        if not first:
                            eng.wait_ge(st3_out[u % 2], due(n - 1, 32 * SLOT_UNITS[u % 2], 0))
                    else:
                        eng.wait_ge(st0_out[u % 2], due(n, 32 * SLOT_UNITS[u % 2], 32 * (u // 2)))
                split_hi(0, n, k, slots(X, R * k, R), staged(k, R, 0))

            def split1(i, k):
                split_hi(1, i, k, slots(X, R * k, R), win(A, R * k, R, 0))

            def split2(i, buf, k):
                s0, n = chunk(k)
                split_hi(2, i, k, slots(X2[buf], s0, n), win(A, s0, n, 0))

            def split3(i, buf, k, front):
                s0, n = chunk(k)
                u = min(k // 2, UNITS - 1)
                if k % 2 == 0 and k // 2 < UNITS:
                    if u < 2:
                        eng.wait_ge(st0_out[u % 2], due(i + 1 if front else i, 32 * SLOT_UNITS[u % 2], 32 * SLOT_UNITS[u % 2]))
                    else:
                        eng.wait_ge(st3_out[u % 2], due(i, 32 * SLOT_UNITS[u % 2], 32 * (u // 2)))
                split_hi(3, i, k, slots(X2[buf], s0, n), staged(k, n, 0))

            def fold(q, i, dst, src):
                eng.wait_ge(gr[q], due(i, RS[q], 2))
                act(dst, src, scale=GN[:, q, 8:9]).then_inc(fh[q], 1)

            def fold1(i):
                eng.wait_ge(fk, due(i, 3, 3))
                act(PKw[:, 0, :], FK[:, :]).then_inc(fh[1], 1)

            def layer1(i, buf, k):
                s0, n = chunk(k)
                eng.wait_ge(l1_mm, due(i, K1, k + 1))
                act(slots(X2[buf], s0, n), bank(PS[k % CB], n * W), bias=GN[:, 1, 3:4], scale=1.0 / KSCALE).then_inc(l1_ev, 1)

            def conv1(i, k):
                eng.wait_ge(c1_mm, due(i, K0, k + 1))
                if k - 1 > 0:
                    eng.wait_ge(c1_lo, due(i, K0, k - 1))
                act2 = PS[k % CB][:, 0:NB]
                nc.scalar.activation(relu[:, k % 2, :], act2, ACT.Relu, bias=PC[:, BB1:BB1 + 1], scale=PC[:, S1:S1 + 1]).then_inc(c1_act, 1)
                act(leak[:, k % 2, :], act2, bias=PC[:, AB1:AB1 + 1], scale=PC[:, AS1:AS1 + 1]).then_inc(c1_act, 1)

            def conv1_hi(i, k):
                eng.wait_ge(c1_h, due(i, K0, k + 1))
                act(win(Hb, R * k, R, 0), relu[:, k % 2, :].rearrange("p (s w) -> p s w", w=W)).then_inc(c1_hi, 1)

            def edges(i, buf, e, first):
                s0, n, stride = (U * e + 1, min(U, HALF - U * e - 1), 1) if e < UNITS else (0, 2, HALF)
                if e == 0:
                    eng.wait_ge(gr[2], due(i, RS[2], RS[2]))
                eng.wait_ge(lo[2], due(i, TC[2], min(2 * e + 3, K1)))
                rows = slots(X2[buf], s0, n, stride)
                act(rows, rows, bias=GN[:, 2, 11:12], scale=GN[:, 2, 9:10]).then_inc(ed_act, 1)
                eng.wait_ge(ed_mm, due(i, EDGES, e + 1))
                if e > 0 or not first:
                    eng.wait_ge(ed_add, due(i, 3 * EDGES, max(0, 3 * e - 1)))
                p = PF[e % 4]
                act(g3[:, 0:n, :], bank(p, n * HALF, HALF), scale=GN[:, 2, 12:13]).then_inc(ed_act, 1)
                act(g1[:, 0:n, 1:HALF + 1], bank(p, n * HALF, HALF), scale=GN[:, 2, 13:14]).then_inc(ed_act, 1)
                for dst, src in ((0, 0), (HALF + 1, HALF - 1)):
                    act(g1[:, 0:n, dst:dst + 1], bass.AP(p, src, [[512, 128], [HALF, n], [1, 1]]), scale=GN[:, 2, 13:14])\
                        .then_inc(ed_act, 1)

            def conv3(b, k):
                s0, n = chunk(k)
                eng.wait_ge(c3_mm, due(b, K1, k + 1))
                if k - 1 > 0:
                    eng.wait_ge(c3_add, due(b, K1, k - 1))
                act(last_tmp[:, k % 2, 0:n * W], PS[k % CB][:, 0:n * W], bias=PR[:, BIAS3:BIAS3 + 1], scale=1.0 / WSCALE)\
                    .then_inc(c3_ev, 1)

            def spectrum_step(b, s):
                inv = 1.0 / MSCALE
                g = s
                if g < FFTS:
                    eng.wait_ge(f_mm[0], due(b, FFTS, g + 1))
                    if g - 1 > 0:
                        eng.wait_ge(f_mm[1], due(b, FFTS, g - 1))
                    act(z1[:, g % 2, 0, :], PF[0][0:W, 0:NB], scale=inv).then_inc(f_hi[0], 1)
                g = s - 1
                if 0 <= g < FFTS:
                    eng.wait_ge(f_mask, due(b, FFTS, g + 1))
                    if g - 1 > 0:
                        eng.wait_ge(f_mm[2], due(b, FFTS, g - 1))
                    act(z2[:, g % 2, 0, :, MASKED:W],
                        bass.AP(PF[1], MASKED, [[512, H], [W, PLANES], [1, W - MASKED]]), scale=inv).then_inc(f_hi[1], 1)
                    act(z2[:, g % 2, 0, :, 0:MASKED], zm[:, g % 2, :, :]).then_inc(f_hi[1], 1)
                g = s - 2
                if 0 <= g < FFTS:
                    eng.wait_ge(f_mm[2], due(b, FFTS, g + 1))
                    if g - 1 > 0:
                        eng.wait_ge(f_mm[3], due(b, FFTS, g - 1))
                    act(z3[:, g % 2, 0, :], PF[2][0:H, 0:NB], scale=inv).then_inc(f_hi[2], 1)
                g = s - 3
                if 0 <= g < FFTS:
                    eng.wait_ge(f_mm[3], due(b, FFTS, g + 1))
                    if 48 * (g // 2) > 0:
                        eng.wait_ge(y_out[g % 2], due(b, 16 * 3 * FFTS // 2, 48 * (g // 2)))
                    act(ystage[:, g % 2, :, 0, 2:W + 2], bank(PF[3], NB, W, H), scale=inv).then_inc(f_hi[3], 1)

            def load_y(b, u):
                if u == 0:
                    for p in range(2):
                        eng.wait_ge(y_out[p], due(b, 16 * 3 * FFTS // 2, 16 * 3 * FFTS // 2))
                if 2 * u - 2 > 0:
                    eng.wait_ge(c3_mm, due(b, K1, 2 * u - 2))
                s0, n = unit(u)
                for par in range(2):
                    src = bass.AP(rowsy.tensor, (2 * s0 + (1 - par)) * YROW, [[YROWS * YROW, C], [2 * YROW, n + 1], [1, YROW]])
                    eng.dma_start(Y[par * C:(par + 1) * C, u % 2, 0:n + 1, :], src).then_inc(y_in[u % 2], 16)

            def iteration(eng, i, buf, back, front):
                n, b = i + 1, i - 1
                for k in range(K1):
                    for c in range(6 + 2 * k, min(8 + 2 * k, K0)):
                        split1(i, c)
                    if back and k == U // R * EARLY:
                        eng.wait_ge(out_late, due(i - 2, 32 * (UNITS - EARLY), 32 * (UNITS - EARLY) + 1))
                    layer1(i, buf, k)
                    if back and k >= FFT_AT:
                        spectrum_step(b, k - FFT_AT)
                if back:
                    spectrum_step(b, STEPS - 7)
                split2(i, buf, 0)
                if back:
                    spectrum_step(b, STEPS - 6)
                split2(i, buf, 1)
                split2(i, buf, 2)
                if back:
                    spectrum_step(b, STEPS - 5)
                fold(2, i, P1w[:, 0, :], M1[:, :])
                if back:
                    spectrum_step(b, STEPS - 4)
                for k in range(3, 7):
                    split2(i, buf, k)
                for k in range(K0):
                    if k + 7 < K1:
                        split2(i, buf, k + 7)
                    conv1(i, k)
                    if k >= 1:
                        conv1_hi(i, k - 1)
                    if back and k < 3:
                        spectrum_step(b, STEPS - 3 + k)
                    if front and 3 <= k < 10:
                        split0(n, 2 * (k - 3), not back)
                        split0(n, 2 * (k - 3) + 1, not back)
                    for e in edges_with(k):
                        edges(i, buf, e, not back)
                conv1_hi(i, K0 - 1)
                if front:
                    fold(0, n, P0w[:, 0, :], M0[:, :])
                if back:
                    fold(3, b, P3w[:, 0, :], M3[:, :])
                if front:
                    eng.wait_ge(a_free, due(n, 1, 1))
                if back:
                    load_y(b, 0)
                    load_y(b, 1)
                if front:
                    gather(eng, offset_reg, range(1, C, 2))
                for k in range(K1):
                    if back:
                        conv3(b, k)
                        if k % 2 == 1 and k // 2 + 2 < UNITS:
                            load_y(b, k // 2 + 2)
                    if front and k == GN1_AT + 3:
                        fold1(n)
                    if front and k == K1 - 2:
                        split1(n, 0)
                        split1(n, 1)
                    for c in split3_with(k):
                        split3(i, buf, c, front)
                if front:
                    for c in range(2, 6):
                        split1(n, c)
                if back:
                    eng.wait_ge(out_early, due(b, 32 * EARLY, 32 * EARLY))

            def tail(eng, b, buf):
                for s in range(STEPS):
                    spectrum_step(b, s)
                fold(3, b, P3w[:, 0, :], M3[:, :])
                load_y(b, 0)
                load_y(b, 1)
                for k in range(K1):
                    conv3(b, k)
                    if k % 2 == 1 and k // 2 + 2 < UNITS:
                        load_y(b, k // 2 + 2)

            eng.wait_ge(const_in, 16 * 12)
            act(P2w[:, 0, :], FK[:, :], scale=W2SCALE).then_inc(setup_a, 1)
            eng.wait_ge(zeroed, 4)
            eng.wait_ge(setup_v, SETUP_V)
            for k in range(K0):
                split0(0, k, True)
            fold(0, 0, P0w[:, 0, :], M0[:, :])
            eng.wait_ge(a_free, 1)
            gather(eng, offset_reg, range(1, C, 2))
            for k in range(6):
                split1(0, k)
            fold1(0)
            program(iteration, tail)(eng)

        @block.vector
        def _(eng):
            v = nc.vector

            def stats(q, i, col, src):
                v.bn_stats(ST[q][:, col, :], src).then_inc(bn[q], 1)

            def flat(t, size, s0, n, p0=0, pn=128):
                return at(t, size, [[1, n * W]], s0 * W, p0, pn)

            def stats0(q, i, k):
                stats(q, i, k, flat(X, HALF * W, R * k, R))

            def stats1(q, i, buf, j):
                size = HALF1 * W
                if j < K0:
                    s0 = R * j + 1
                    stats(q, i, j, flat(X2[buf], size, s0, min(R, HALF - s0)))
                else:
                    v.bn_stats(ST[q][0:C, K0, :], flat(X2[buf], size, 0, 1, 0, C)).then_inc(bn[q], 1)
                    v.bn_stats(ST[q][C:2 * C, K0, :], flat(X2[buf], size, HALF, 1, C, C)).then_inc(bn[q], 1)

            def aggregate(q, i):
                eng.wait_ge(bn[q], due(i, BN[q], BN[q]))
                v.tensor_copy(GN[:, q, 14:15], ST[q][:, 0, 0:1])
                chunks = K0 if q < 2 else K1
                v.bn_aggr(GN[:, q, 0:2], ST[q][:, 0:chunks, :].rearrange("p k s -> p (k s)")).then_inc(gv[q], 1)

            def center(q, i):
                eng.wait_ge(gp[q], due(i, 2, 1))
                p = PSS[:, 2 * q:2 * q + 1]
                v.tensor_scalar(GN[:, q, 2:3], p, -1.0, None, ALU.mult).then_inc(gv[q], 1)
                v.tensor_copy(GN[:, q, 3:4], p).then_inc(gv[q], 1)
                eng.wait_ge(gv[q], due(i, 6, 2))
                v.tensor_tensor(GN[:, q, 4:5], GN[:, q, 0:1], GN[:, q, 2:3], ALU.add).then_inc(gv[q], 1)
                eng.wait_ge(gv[q], due(i, 6, 4))
                v.scalar_tensor_tensor(GN[:, q, 5:6], GN[:, q, 4:5], GN[:, q, 4:5], GN[:, q, 1:2],
                                       op0=ALU.mult, op1=ALU.add).then_inc(gv[q], 1)

            def variance(q, i):
                eng.wait_ge(gp[q], due(i, 2, 2))
                v.tensor_scalar(GN[:, q, 6:7], PSS[:, 2 * q + 1:2 * q + 2], EPS, None, ALU.add).then_inc(gv[q], 1)

            def split_lo(q, i, k, src, dst, hi_part):
                eng.wait_ge(hi[q], due(i, TC[q], k + 1))
                v.scalar_tensor_tensor(dst, src, GN[:, q, 2:3], hi_part, op0=ALU.add, op1=ALU.subtract).then_inc(lo[q], 1)

            def staged(k, n, part):
                u = min(k // 2, UNITS - 1)
                return stage[:, u % 2, R * k - U * u:R * k - U * u + n, part * PITCH:part * PITCH + W]

            def split0(n, k):
                split_lo(0, n, k, slots(X, R * k, R), staged(k, R, 1), staged(k, R, 0))

            def split1(i, k):
                split_lo(1, i, k, slots(X, R * k, R), win(A, R * k, R, 1), win(A, R * k, R, 0))

            def split2(i, buf, k):
                s0, n = chunk(k)
                split_lo(2, i, k, slots(X2[buf], s0, n), win(A, s0, n, 1), win(A, s0, n, 0))
                if k == 0:
                    eng.wait_ge(lo[2], due(i, TC[2], 1))
                    v.memset(at(A, ASIZE, [[1, ROW]], FRONT + ROW, C, C), 0.0).then_inc(t2_zero, 1)
                if k == K1 - 1:
                    eng.wait_ge(lo[2], due(i, TC[2], K1))
                    v.memset(at(A, ASIZE, [[1, ROW]], FRONT + (HALF + 1) * ROW, 0, C), 0.0).then_inc(t2_zero, 1)

            def split3(i, buf, k):
                s0, n = chunk(k)
                split_lo(3, i, k, slots(X2[buf], s0, n), staged(k, n, 1), staged(k, n, 0))

            def fold(q, i, dst, src, hi_part):
                eng.wait_ge(fh[q], due(i, 1, 1))
                v.scalar_tensor_tensor(dst, src, GN[:, q, 8:9], hi_part, op0=ALU.mult, op1=ALU.subtract).then_inc(fl[q], 1)

            def fold1(i):
                eng.wait_ge(gr[1], due(i, RS[1], 2))
                r = GN[:, 1, 8:9]
                v.tensor_scalar(FK[:, 0:256], MK[:, 0:256], r, None, ALU.mult).then_inc(fk, 1)
                v.tensor_scalar(FK[:, 512:768], MK[:, 512:768], r, None, ALU.mult).then_inc(fk, 1)
                v.scalar_tensor_tensor(FK[:, 256:512], MK[:, 256:512], r, D1[:, :], op0=ALU.mult, op1=ALU.add).then_inc(fk, 1)

            def fold1_lo(i):
                eng.wait_ge(fh[1], due(i, 1, 1))
                v.tensor_tensor(PKw[:, 1, :], FK[:, :], PKw[:, 0, :], ALU.subtract).then_inc(fl[1], 1)

            def layer0(i, k):
                eng.wait_ge(l0_mm, due(i, K0, k + 1))
                v.scalar_tensor_tensor(slots(X, R * k, R), bank(PF[k % 4]), PR[:, BIAS0:BIAS0 + 1], slots(X, R * k, R),
                                       op0=ALU.add, op1=ALU.add).then_inc(l0_ev, 1)

            def conv1_h(i, k):
                eng.wait_ge(c1_act, due(i, 2 * K0, 2 * k + 2))
                v.scalar_tensor_tensor(relu[:, k % 2, :], relu[:, k % 2, :], PC[:, OMA:OMA + 1], leak[:, k % 2, :],
                                       op0=ALU.mult, op1=ALU.add).then_inc(c1_h, 1)

            def conv1_lo(i, k):
                eng.wait_ge(c1_hi, due(i, K0, k + 1))
                v.tensor_tensor(win(Hb, R * k, R, 1), relu[:, k % 2, :].rearrange("p (s w) -> p s w", w=W),
                                win(Hb, R * k, R, 0), ALU.subtract).then_inc(c1_lo, 1)

            def conv2(i, buf, k):
                s0, n = chunk(k)
                if k == 0:
                    eng.wait_ge(ed_add, due(i, 3 * EDGES, 3 * EDGES))
                eng.wait_ge(c2_mm, due(i, K1, k + 1))
                rows = slots(X2[buf], s0, n)
                v.scalar_tensor_tensor(rows, bank(PS[k % CB], n * W), PC[:, S2:S2 + 1], rows, op0=ALU.mult, op1=ALU.add)\
                    .then_inc(c2_ev, 1)

            def spectrum_step(b, s):
                inv = 1.0 / MSCALE
                g = s
                if g < FFTS:
                    eng.wait_ge(f_hi[0], due(b, FFTS, g + 1))
                    v.scalar_tensor_tensor(z1[:, g % 2, 1, :], PF[0][0:W, 0:NB], inv, z1[:, g % 2, 0, :],
                                           op0=ALU.mult, op1=ALU.subtract).then_inc(f_lo[0], 1)
                g = s - 1
                if 0 <= g < FFTS:
                    eng.wait_ge(f_mm[1], due(b, FFTS, g + 1))
                    v.tensor_tensor(zm[:, g % 2, :, :], bass.AP(PF[1], 0, [[512, H], [W, PLANES], [1, MASKED]]),
                                    bass.AP(MA, 0, [[MASKED, H], [0, PLANES], [1, MASKED]]), ALU.mult).then_inc(f_mask, 1)
                    eng.wait_ge(f_hi[1], due(b, 2 * FFTS, 2 * g + 1))
                    v.scalar_tensor_tensor(z2[:, g % 2, 1, :, MASKED:W],
                                           bass.AP(PF[1], MASKED, [[512, H], [W, PLANES], [1, W - MASKED]]), inv,
                                           z2[:, g % 2, 0, :, MASKED:W], op0=ALU.mult, op1=ALU.subtract).then_inc(f_lo[1], 1)
                    eng.wait_ge(f_hi[1], due(b, 2 * FFTS, 2 * g + 2))
                    v.tensor_tensor(z2[:, g % 2, 1, :, 0:MASKED], zm[:, g % 2, :, :], z2[:, g % 2, 0, :, 0:MASKED],
                                    ALU.subtract).then_inc(f_lo[1], 1)
                g = s - 2
                if 0 <= g < FFTS:
                    eng.wait_ge(f_hi[2], due(b, FFTS, g + 1))
                    v.scalar_tensor_tensor(z3[:, g % 2, 1, :], PF[2][0:H, 0:NB], inv, z3[:, g % 2, 0, :],
                                           op0=ALU.mult, op1=ALU.subtract).then_inc(f_lo[2], 1)
                g = s - 3
                if 0 <= g < FFTS:
                    eng.wait_ge(f_hi[3], due(b, FFTS, g + 1))
                    v.scalar_tensor_tensor(ystage[:, g % 2, :, 1, 2:W + 2], bank(PF[3], NB, W, H), inv,
                                           ystage[:, g % 2, :, 0, 2:W + 2], op0=ALU.mult, op1=ALU.subtract).then_inc(f_lo[3], 1)

            def layer0_stats(i, chunks):
                for k in chunks:
                    layer0(i, k)
                    if k >= 1:
                        eng.wait_ge(l0_ev, due(i, K0, k))
                        stats0(1, i, k - 1)
                    if k == K0 - 1:
                        eng.wait_ge(l0_ev, due(i, K0, K0))
                        stats0(1, i, K0 - 1)
                        aggregate(1, i)

            def iteration(eng, i, buf, back, front):
                n, b = i + 1, i - 1
                for k in range(K1):
                    for c in range(6 + 2 * k, min(8 + 2 * k, K0)):
                        split1(i, c)
                    if front and k >= 8:
                        for c in range(2 * (k - 8), min(2 * (k - 8) + 2, K0)):
                            if c % 2 == 0:
                                eng.wait_ge(x_in[c // 2], due(n, 32, 32))
                            stats0(0, n, c)
                    if k >= 2:
                        eng.wait_ge(l1_ev, due(i, K1, k))
                        stats1(2, i, buf, k - 2)
                    if back and k >= FFT_AT:
                        spectrum_step(b, k - FFT_AT)
                eng.wait_ge(l1_ev, due(i, K1, K1))
                stats1(2, i, buf, K0 - 1)
                stats1(2, i, buf, K0)
                aggregate(2, i)
                if back:
                    spectrum_step(b, STEPS - 7)
                center(2, i)
                split2(i, buf, 0)
                if back:
                    spectrum_step(b, STEPS - 6)
                variance(2, i)
                split2(i, buf, 1)
                if back:
                    spectrum_step(b, STEPS - 5)
                fold(2, i, P1w[:, 1, :], M1[:, :], P1w[:, 0, :])
                split2(i, buf, 2)
                if back:
                    spectrum_step(b, STEPS - 4)
                split2(i, buf, 3)
                if front:
                    aggregate(0, n)
                for k in range(K0):
                    if 4 + k < K1:
                        split2(i, buf, 4 + k)
                    if back and k < 3:
                        spectrum_step(b, STEPS - 3 + k)
                    conv1_h(i, k)
                    if k >= 1:
                        conv1_lo(i, k - 1)
                    if front and k == 2:
                        center(0, n)
                    if front and k == 4:
                        variance(0, n)
                    if front and 3 <= k < 10:
                        split0(n, 2 * (k - 3))
                        split0(n, 2 * (k - 3) + 1)
                conv1_lo(i, K0 - 1)
                if front:
                    fold(0, n, P0w[:, 1, :], M0[:, :], P0w[:, 0, :])
                if back:
                    fold(3, b, P3w[:, 1, :], M3[:, :], P3w[:, 0, :])
                for k in range(K1):
                    conv2(i, buf, k)
                    if k >= 1:
                        eng.wait_ge(c2_ev, due(i, K1, k))
                    if k >= 2:
                        stats1(3, i, buf, k - 2)
                eng.wait_ge(c2_ev, due(i, K1, K1))
                stats1(3, i, buf, K0 - 1)
                stats1(3, i, buf, K0)
                aggregate(3, i)
                for k in range(K1):
                    if k == 2:
                        center(3, i)
                    if front:
                        layer0_stats(n, layer0_with(k))
                        if k == GN1_AT + 1:
                            center(1, n)
                        if k == GN1_AT + 2:
                            variance(1, n)
                        if k == GN1_AT + 3:
                            fold1(n)
                        if k == GN1_AT + 4:
                            fold1_lo(n)
                    if front and k == K1 - 2:
                        split1(n, 0)
                        split1(n, 1)
                    for c in split3_with(k):
                        split3(i, buf, c)
                    if k == 2:
                        variance(3, i)
                if front:
                    for c in range(2, 6):
                        split1(n, c)

            def tail(eng, b, buf):
                for s in range(STEPS):
                    spectrum_step(b, s)
                fold(3, b, P3w[:, 1, :], M3[:, :], P3w[:, 0, :])

            eng.wait_ge(offs_in, 16)
            eng.wait_ge(const_in, 16 * 12)

            def pc(c):
                return PC[:, c:c + 1]

            def pr(c):
                return PR[:, c:c + 1]

            for c, value in ((HALFM, -0.5), (ONE, 1.0), (KS, KSCALE), (WS, WSCALE)):
                v.memset(pc(c), value).then_inc(setup_v, 1)
            v.tensor_scalar(pc(VE1), pr(V1), EPS, None, ALU.add).then_inc(setup_v, 1)
            v.tensor_scalar(pc(VE2), pr(V2), EPS, None, ALU.add).then_inc(setup_v, 1)
            v.tensor_scalar(OFFB[:, :], OFFI[:, :], float(-REACH), float(REACH), ALU.max, ALU.min).then_inc(setup_v, 1)
            eng.wait_ge(setup_v, 7)
            v.scalar_tensor_tensor(OFFI[:, 0:C], OFFB[:, 0:2 * C:2], float(ROW), OFFB[:, 1:2 * C:2],
                                        op0=ALU.mult, op1=ALU.add).then_inc(setup_v, 1)
            eng.wait_ge(setup_v, 8)
            v.tensor_scalar(OFF[:, :], OFFI[:, 0:C], float(REACH * ROW + GUARD), None, ALU.add).then_inc(setup_v, 1)
            eng.wait_ge(setup_p, 2)
            v.tensor_tensor(pc(S1), pr(G1), pc(RT1), ALU.mult).then_inc(setup_v, 1)
            v.tensor_tensor(pc(S2), pr(G2), pc(RT2), ALU.mult).then_inc(setup_v, 1)
            v.tensor_tensor(pc(BB1), pr(B1), pr(MM1), ALU.subtract).then_inc(setup_v, 1)
            v.tensor_tensor(pc(BB2), pr(B2), pr(MM2), ALU.subtract).then_inc(setup_v, 1)
            v.tensor_scalar(pc(OMA), pr(ALPHA), -1.0, 1.0, ALU.mult, ALU.add).then_inc(setup_v, 1)
            eng.wait_ge(setup_v, 14)
            v.scalar_tensor_tensor(pc(BB1), pc(BB1), pc(S1), pr(BE1), op0=ALU.mult, op1=ALU.add).then_inc(setup_v, 1)
            v.scalar_tensor_tensor(pc(BB2), pc(BB2), pc(S2), pr(BE2), op0=ALU.mult, op1=ALU.add).then_inc(setup_v, 1)
            eng.wait_ge(setup_v, 16)
            v.tensor_scalar(pc(S1), pc(S1), 1.0 / WSCALE, None, ALU.mult).then_inc(setup_v, 1)
            v.tensor_scalar(pc(S2), pc(S2), 1.0 / W2SCALE, None, ALU.mult).then_inc(setup_v, 1)
            eng.wait_ge(setup_v, 18)
            v.tensor_tensor(pc(AS1), pc(S1), pr(ALPHA), ALU.mult).then_inc(setup_v, 1)
            v.tensor_tensor(pc(AB1), pc(BB1), pr(ALPHA), ALU.mult).then_inc(setup_v, 1)
            eng.wait_ge(setup_a, 1)
            v.scalar_tensor_tensor(P2w[:, 1, :], FK[:, :], W2SCALE, P2w[:, 0, :], op0=ALU.mult, op1=ALU.subtract).then_inc(setup_v, 1)
            eng.wait_ge(setup_v, 21)
            for k in range(K0):
                if k % 2 == 0:
                    eng.wait_ge(x_in[k // 2], 32)
                stats0(0, 0, k)
            aggregate(0, 0)
            center(0, 0)
            variance(0, 0)
            for k in range(K0):
                split0(0, k)
            fold(0, 0, P0w[:, 1, :], M0[:, :], P0w[:, 0, :])
            layer0_stats(0, range(K0))
            center(1, 0)
            variance(1, 0)
            fold1(0)
            for k in range(6):
                split1(0, k)
            fold1_lo(0)
            program(iteration, tail)(eng)

        @block.gpsimd
        def _(eng):
            g_ = nc.gpsimd
            scale_of = [ONE, KS, WS, WS]

            def inverse(q, i):
                eng.wait_ge(gv[q], due(i, 6, 6))
                g_.tensor_tensor(GN[:, q, 7:8], GN[:, q, 6:7], PC[:, HALFM:HALFM + 1], ALU.pow).then_inc(gr[q], 1)
                eng.wait_ge(gr[q], due(i, RS[q], 1))
                s = scale_of[q]
                g_.tensor_tensor(GN[:, q, 8:9], GN[:, q, 7:8], PC[:, s:s + 1], ALU.mult).then_inc(gr[q], 1)

            def layer2_scales(i):
                r = GN[:, 2, 7:8]
                g_.tensor_scalar(GN[:, 2, 9:10], r, 1.0, None, ALU.add).then_inc(gr[2], 1)
                g_.tensor_tensor(GN[:, 2, 10:11], r, GN[:, 2, 2:3], ALU.mult).then_inc(gr[2], 1)
                g_.tensor_scalar(GN[:, 2, 12:13], r, 0.75, None, ALU.mult).then_inc(gr[2], 1)
                g_.tensor_scalar(GN[:, 2, 13:14], r, 0.25, None, ALU.mult).then_inc(gr[2], 1)
                eng.wait_ge(gr[2], due(i, RS[2], 6))
                g_.tensor_tensor(GN[:, 2, 11:12], GN[:, 2, 10:11], PC[:, BB2:BB2 + 1], ALU.add).then_inc(gr[2], 1)

            def restore_zeros(i):
                for part in range(2):
                    g_.memset(win(A, 0, HALF, part, W, 1, PADS), 0.0).then_inc(pads, 1)
                g_.memset(at(A, ASIZE, [[1, ROW]], FRONT + (HALF + 1) * ROW), 0.0).then_inc(pads, 1)

            def edges(i, buf, e):
                s0, n, stride = (U * e + 1, min(U, HALF - U * e - 1), 1) if e < UNITS else (0, 2, HALF)
                eng.wait_ge(ed_act, due(i, 5 * EDGES, 5 * e + 5))
                if e > 0:
                    eng.wait_ge(ed_add, due(i, 3 * EDGES, 3 * e))
                g_.tensor_tensor(ebuf[:, 0:n, :, 0], g3[:, 0:n, :], g1[:, 0:n, 0:HALF], ALU.add).then_inc(ed_add, 1)
                g_.tensor_tensor(ebuf[:, 0:n, :, 1], g3[:, 0:n, :], g1[:, 0:n, 2:HALF + 2], ALU.add).then_inc(ed_add, 1)
                eng.wait_ge(ed_add, due(i, 3 * EDGES, 3 * e + 2))
                rows = slots(X2[buf], s0, n, stride)
                g_.tensor_tensor(rows, rows, ebuf[:, 0:n, :, :].rearrange("p s j q -> p s (j q)"), ALU.add).then_inc(ed_add, 1)

            def conv3(b, buf, k):
                s0, n = chunk(k)
                eng.wait_ge(c3_ev, due(b, K1, k + 1))
                rows = slots(X2[buf], s0, n)
                g_.tensor_tensor(rows, rows, last_tmp[:, k % 2, 0:n * W].rearrange("p (s w) -> p s w", w=W), ALU.add)\
                    .then_inc(c3_add, 1)

            def wrap(b, g):
                eng.wait_ge(f_lo[3], due(b, FFTS, g + 1))
                last = ystage[:, g % 2, :, :, W:W + 2].rearrange("h c p e -> h (c p) e")
                ones = bass.AP(PC, ONE, [[16, H], [0, 2 * PLANES], [0, 2]])
                g_.tensor_tensor(ystage[:, g % 2, :, :, 0:2].rearrange("h c p e -> h (c p) e"), last, ones, ALU.mult)\
                    .then_inc(y_wrap, 1)

            def iteration(eng, i, buf, back, front):
                n, b = i + 1, i - 1
                if back:
                    for g in range(FFTS):
                        wrap(b, g)
                        if g == FFTS - 6:
                            inverse(2, i)
                            layer2_scales(i)
                else:
                    inverse(2, i)
                    layer2_scales(i)
                for k in range(K0):
                    if front and k == 4:
                        inverse(0, n)
                    for e in edges_with(k):
                        edges(i, buf, e)
                for k in range(K1):
                    if k == 3:
                        inverse(3, i)
                    if front and k == GN1_AT + 2:
                        inverse(1, n)
                        restore_zeros(n)
                    if back:
                        conv3(b, 1 - buf, k)

            def tail(eng, b, buf):
                for g in range(FFTS):
                    wrap(b, g)
                for k in range(K1):
                    conv3(b, buf, k)

            g_.memset(A[:, :], 0.0).then_inc(zeroed, 1)
            g_.memset(Hb[:, :], 0.0).then_inc(zeroed, 1)
            g_.memset(stage[:, :, :, :], 0.0).then_inc(zeroed, 1)
            g_.memset(GN[:, :, :], 0.0).then_inc(zeroed, 1)
            eng.wait_ge(setup_v, 6)
            g_.tensor_tensor(PC[:, RT1:RT1 + 1], PC[:, VE1:VE1 + 1], PC[:, HALFM:HALFM + 1], ALU.pow).then_inc(setup_p, 1)
            g_.tensor_tensor(PC[:, RT2:RT2 + 1], PC[:, VE2:VE2 + 1], PC[:, HALFM:HALFM + 1], ALU.pow).then_inc(setup_p, 1)
            inverse(0, 0)
            inverse(1, 0)
            restore_zeros(0)
            program(iteration, tail)(eng)


def pair_matrices(w, rows_in, rows_out, tap):
    m = np.zeros((128, 3, 2, 128), np.float32)
    for which in range(2):
        for pi in range(2):
            for po in range(2):
                kh = tap(rows_in[which][pi], rows_out[po])
                if 0 <= kh < 3:
                    for kw in range(3):
                        m[64 * pi:64 * pi + 64, kw, which, 64 * po:64 * po + 64] = w[kh][kw]
    return m.reshape(128, 768)


def spectrum_matrices():
    freqs = [("c", a) for a in range(26, 57)] + [("s", a) for a in range(26, 56)]
    freqs += [("c", a) for a in range(26)] + [("s", a) for a in range(1, 26)]
    vs = [("c", a) for a in range(57)] + [("s", a) for a in range(1, 56)]
    h, ang = np.arange(H), 2 * np.pi / H

    def wave(kind, a):
        return (np.cos if kind == "c" else np.sin)(ang * (a * h % H))

    fa = np.array([wave(k, 56 - a) * (1 if k == "c" else -1) for k, a in freqs])
    fb = np.array([wave(k, (a - 28) % 57) for k, a in vs])
    fl_ = np.array([wave(k, a) * (1 if a in (0, 56) else 2) for k, a in freqs])
    fr = np.array([wave(k, a) * (1 if a in (0, 56) else 2) for k, a in vs])
    m = np.array([fa.T, fb.T, fr, fl_]) * (MSCALE / np.sqrt(H))
    parts = np.zeros((H, 4, 2, W), np.float16)
    for n in range(4):
        parts[:, n, 0] = m[n].astype(np.float16)
        parts[:, n, 1] = (m[n] - parts[:, n, 0].astype(np.float64)).astype(np.float16)
    mask = np.array([[0.0 if (56 - a) ** 2 + (56 - b) ** 2 <= 900 else 1 / MSCALE for _, a in freqs[:MASKED]]
                     for _, b in vs], np.float32)
    return parts, mask


def edge_matrices():
    eye = np.eye(64)
    coef = {(0, 0): 1.5, (0, 1): -0.5, (1, 0): -0.5, (1, 1): -0.5}
    inner = np.zeros((128, 6, 128), np.float16)
    ends = np.zeros((128, 8, 128), np.float16)
    towards = {(0, 0): (0.25, 0.75), (1, 0): (0.75, 0.25), (1, 1): (0.25, 0.75), (2, 1): (0.75, 0.25)}
    for (which, pi), ws in towards.items():
        for col in range(2):
            for po in range(2):
                inner[64 * pi:64 * pi + 64, 2 * which + col, 64 * po:64 * po + 64] = eye * (coef[pi, col] * ws[po])
    for end in range(2):
        for pi in range(2):
            for col in range(2):
                ends[64 * pi:64 * pi + 64, 4 * end + 2 * pi + col, 64 * end:64 * end + 64] = eye * coef[pi, col]
    return inner, ends


def kernel(x, L0_conv_weight, L0_conv_bias, L0_conv_offsets, L1_conv_K, L2_conv_w1, L2_conv_b1, L2_conv_g1,
           L2_conv_be1, L2_conv_m1, L2_conv_v1, L2_conv_a_prelu, L2_conv_w2, L2_conv_b2, L2_conv_g2, L2_conv_be2,
           L2_conv_m2, L2_conv_v2, L3_conv_weight, L3_conv_bias):
    import concourse.bacc as bacc
    from concourse.bass_utils import run_bass_kernel_spmd

    def array(a):
        return np.asarray(a)

    w0 = np.zeros((128, 128), np.float32)
    w0[:64, :64] = w0[64:, 64:] = array(L0_conv_weight)
    kk = array(L1_conv_K)
    diag = np.zeros((3, 3, 64, 64), np.float32)
    for c in range(64):
        diag[:, :, c, c] = kk
    p0_p1 = (((-2, -1), (0, 1)), (0, -1))
    p1_p0 = (((0, -1), (2, 1)), (0, 1))
    p1_p1 = (((-2, -3), (0, -1)), (0, -1))

    def same(h_in, h_out):
        return h_in - h_out + 1

    def causal(h_in, h_out):
        return h_out - h_in

    w1, w2, w3 = (np.transpose(array(w), (2, 3, 1, 0)) for w in (L2_conv_w1, L2_conv_w2, L3_conv_weight))
    delta = np.zeros((128, 2, 128), np.float32)
    delta[:64, 1, :64] = delta[64:, 0, 64:] = KSCALE * np.eye(64)
    average = np.zeros((128, 128), np.float32)
    for p in range(128):
        for q in range(128):
            if p % 64 // 2 == q % 64 // 2:
                average[p, q] = 0.25
    params = np.zeros((128, 13), np.float32)
    for n, a in enumerate((L0_conv_bias, L2_conv_g1, L2_conv_be1, L2_conv_m1, L2_conv_v1, L2_conv_b1, L2_conv_g2,
                           L2_conv_be2, L2_conv_m2, L2_conv_v2, L2_conv_b2, L3_conv_bias)):
        params[:64, n] = params[64:, n] = array(a)
    params[:, 12] = array(L2_conv_a_prelu)[0]
    edge, edge_ends = edge_matrices()
    spectrum, mask = spectrum_matrices()
    arrays = {
        "x": np.ascontiguousarray(array(x)), "offsets": np.ascontiguousarray(array(L0_conv_offsets)).reshape(1, 128),
        "w0": w0, "k1": pair_matrices(diag, *p0_p1, same),
        "delta": delta.reshape(128, 256), "w1": pair_matrices(w1, *p1_p0, same), "w2": pair_matrices(w2, *p0_p1, same),
        "w3": pair_matrices(w3, *p1_p1, causal), "params": params, "average": average, "edge": edge,
        "edge_ends": edge_ends, "spectrum": spectrum, "mask": mask,
    }
    nc = bacc.Bacc("TRN2", target_bir_lowering=False, num_devices=1, dynamic_dma_scratch_size=1024)
    aps = {n: nc.dram_tensor(n, a.shape, mybir.dt.from_np(a.dtype), kind="ExternalInput").ap() for n, a in arrays.items()}
    aps["out"] = nc.dram_tensor("out", (N, C, H, W), F32, kind="ExternalOutput").ap()
    build(nc, **aps)
    done = run_bass_kernel_spmd(nc, [arrays], core_ids=[0])
    return done.results[0]["out"]
```
